# Optimizing a Trainium2 kernel written in Bass

```python
import numpy as np
import jax
import jax.numpy as jnp

def _softmax(x, axis=-1):
    return jax.nn.softmax(x, axis=axis)

def _gelu(x):
    return jax.nn.gelu(x, approximate=True)

def _silu(x):
    return jax.nn.silu(x)

def _sigmoid(x):
    return jax.nn.sigmoid(x)

def _layernorm(x, axis=-1, eps=1e-05):
    m = jnp.mean(x, axis=axis, keepdims=True)
    v = jnp.var(x, axis=axis, keepdims=True)
    return (x - m) / jnp.sqrt(v + eps)

def _scatter_add(tgt, idx, src, axis=0):
    return tgt.at[idx].add(src)

def _segment_sum(src, seg, n):
    return jax.ops.segment_sum(src, seg, n)
kernel_name = 'mk_adj_preln_d1_adj_r2_90cc14'

def setup_inputs(seed: int=0):
    np.random.seed(seed)
    _w = jnp.asarray

    def _rec_inputs():
        import jax
        import jax.numpy as jnp
        _gk = jax.random.key(seed)
        x = 7.22e-05 + 1 * jax.random.normal(jax.random.fold_in(_gk, 1), (16, 512, 256), jnp.float32)
        _a = jax.random.bernoulli(jax.random.fold_in(_gk, 2), 0.015625, (512, 512))
        _a = jnp.logical_or(_a, jnp.swapaxes(_a, -1, -2))
        _a = jnp.logical_or(_a, jnp.eye(512, dtype=bool))
        _af = _a.astype(jnp.float32)
        _af = _af * jax.random.uniform(jax.random.fold_in(_gk, 3), (512, 512), jnp.float32, 0.05, 0.00390622)
        adj = _af
        return (x, adj)
    x, adj = _rec_inputs()

    def _L0_gnn_setup():
        import jax, jax.numpy as jnp
        import numpy as np
        B, N, D, T = (64, 128, 256, 3)

        def _lin(v, W, b):
            return jnp.einsum('...i,oi->...o', v, W) + b
        key = jax.random.key(seed)
        ks = jax.random.split(key, 12)
        s2 = 1.0 / np.sqrt(2 * D)
        s1 = 1.0 / np.sqrt(D)
        return {'x': jax.random.normal(ks[0], (B, N, D), jnp.float32), 'in_mat': jax.random.uniform(ks[1], (N, N), jnp.float32) / N, 'out_mat': jax.random.uniform(ks[2], (N, N), jnp.float32) / N, 'w3_w': jax.random.normal(ks[3], (D, 2 * D), jnp.float32) * s2, 'w3_b': jnp.zeros((D,), jnp.float32), 'u3_w': jax.random.normal(ks[4], (D, D), jnp.float32) * s1, 'u3_b': jnp.zeros((D,), jnp.float32), 'w4_w': jax.random.normal(ks[5], (D, 2 * D), jnp.float32) * s2, 'w4_b': jnp.zeros((D,), jnp.float32), 'w5_w': jax.random.normal(ks[6], (D, 2 * D), jnp.float32) * s2, 'w5_b': jnp.zeros((D,), jnp.float32), 'u5_w': jax.random.normal(ks[7], (D, D), jnp.float32) * s1, 'u5_b': jnp.zeros((D,), jnp.float32)}
    _L0_gnn_all = _L0_gnn_setup()
    _L0_gnn_in = {k: v for k, v in _L0_gnn_all.items() if k in ('w3_w', 'w3_b', 'u3_w', 'u3_b', 'w4_w', 'w4_b', 'w5_w', 'w5_b', 'u5_w', 'u5_b')}
    del _L0_gnn_all
    return {'x': x, 'adj': adj, 'L0_gnn_w3_w': _L0_gnn_in['w3_w'], 'L0_gnn_w3_b': _L0_gnn_in['w3_b'], 'L0_gnn_u3_w': _L0_gnn_in['u3_w'], 'L0_gnn_u3_b': _L0_gnn_in['u3_b'], 'L0_gnn_w4_w': _L0_gnn_in['w4_w'], 'L0_gnn_w4_b': _L0_gnn_in['w4_b'], 'L0_gnn_w5_w': _L0_gnn_in['w5_w'], 'L0_gnn_w5_b': _L0_gnn_in['w5_b'], 'L0_gnn_u5_w': _L0_gnn_in['u5_w'], 'L0_gnn_u5_b': _L0_gnn_in['u5_b']}

def reference(x, adj, L0_gnn_w3_w, L0_gnn_w3_b, L0_gnn_u3_w, L0_gnn_u3_b, L0_gnn_w4_w, L0_gnn_w4_b, L0_gnn_w5_w, L0_gnn_w5_b, L0_gnn_u5_w, L0_gnn_u5_b):
    import jax
    import jax.numpy as jnp

    def _L0_gnn_ref(x, in_mat, out_mat, w3_w, w3_b, u3_w, u3_b, w4_w, w4_b, w5_w, w5_b, u5_w, u5_b):
        import jax, jax.numpy as jnp
        import numpy as np
        B, N, D, T = (64, 128, 256, 3)

        def _lin(v, W, b):
            return jnp.einsum('...i,oi->...o', v, W) + b
        h = x
        for _ in range(T):
            a_in = jnp.einsum('nm,bmd->bnd', in_mat, h)
            a_out = jnp.einsum('nm,bmd->bnd', out_mat, h)
            av = jnp.concatenate([a_in, a_out], axis=-1)
            z = jax.nn.sigmoid(_lin(av, w3_w, w3_b) + _lin(h, u3_w, u3_b))
            r = jax.nn.sigmoid(_lin(av, w4_w, w4_b) + _lin(h, u3_w, u3_b))
            hv = jnp.tanh(_lin(av, w5_w, w5_b) + _lin(r * h, u5_w, u5_b))
            h = (1.0 - z) * h + z * hv
        return h
    h = jnp.maximum(_layernorm(x, axis=-1), 0.0)
    x = x + _L0_gnn_ref(h, adj, adj, L0_gnn_w3_w, L0_gnn_w3_b, L0_gnn_u3_w, L0_gnn_u3_b, L0_gnn_w4_w, L0_gnn_w4_b, L0_gnn_w5_w, L0_gnn_w5_b, L0_gnn_u5_w, L0_gnn_u5_b)
    return x

_drawn_inputs = setup_inputs


def setup_inputs(seed=0):
    import zlib

    import numpy as np

    out = dict(_drawn_inputs(seed))
    spreads = {'L0_gnn_w3_b': (0.0, 0.535),
     'L0_gnn_u3_b': (0.0, 0.457),
     'L0_gnn_w4_b': (0.0, 0.8),
     'L0_gnn_w5_b': (0.0, 0.1),
     'L0_gnn_u5_b': (0.0, 0.1)}
    factors = {'L0_gnn_w4_w': 3.362}
    for name, (base, spread) in spreads.items():
        noise = np.random.default_rng([zlib.crc32(name.encode()), seed]).standard_normal(out[name].shape)
        drawn = base * np.exp(spread * noise) if base else spread * noise
        out[name] = jnp.asarray(drawn.astype(out[name].dtype))
    for name, factor in factors.items():
        out[name] = (out[name] * factor).astype(out[name].dtype)
    return out
```

```python
from contextlib import ExitStack

import concourse.bass as bass
from concourse import mybir

F32 = mybir.dt.float32
F32R = mybir.dt.float32r
ALU = mybir.AluOpType
ACT = mybir.ActivationFunctionType

P = 128
NB = 512
STEPS = 3
SETS = 2
UNITS = STEPS * SETS
EPS = 1e-5


def gated_graph_network(nc, x, adj, w3_w, w3_b, u3_w, u3_b, w4_w, w4_b, w5_w, w5_b, u5_w, u5_b, out):
    B, N, D = x.shape
    M = N // P
    C = D // P
    PAIRS = B // SETS

    ctx = ExitStack()
    with ctx:
        def sb(name, shape, dt=F32):
            return ctx.enter_context(nc.sbuf_tensor(name, shape, dt))

        def sem(name):
            return ctx.enter_context(nc.semaphore(name))

        ident = sb("ident", [P, P])
        adj_rows = sb("adj_rows", [P, M, N])
        adjT_hi, adjT_lo = sb("adjT_hi", [P, M, N], F32R), sb("adjT_lo", [P, M, N], F32R)
        w_rows = {n: sb(f"{n}_rows", [P, C, 2 * D]) for n in ("w4", "w3", "w5")}
        w_rows |= {n: sb(f"{n}_rows", [P, C, D]) for n in ("u3", "u5")}
        wT_hi = {n: sb(f"{n}T_hi", [P, C, D], F32R) for n in w_rows}
        wT_lo = {n: sb(f"{n}T_lo", [P, C, D], F32R) for n in w_rows}
        bias_rows = sb("bias_rows", [5 * C, P])
        bias_cols = sb("bias_cols", [P, 5, C])
        gate_bias = sb("gate_bias", [P, 3, C])
        x_in = [sb(f"x_in{s}", [P, M, D]) for s in range(SETS)]
        x_out = [sb(f"x_out{s}", [P, M, D]) for s in range(SETS)]
        h_first = [sb(f"h_first{s}", [P, M, D]) for s in range(SETS)]
        hn_hi = [sb(f"hn_hi{s}", [P, M, D], F32R) for s in range(SETS)]
        hn_lo = [sb(f"hn_lo{s}", [P, M, D], F32R) for s in range(SETS)]
        hf = [sb(f"hf{s}", [P, C, N]) for s in range(SETS)]
        hf_hi = [sb(f"hf_hi{s}", [P, C, N], F32R) for s in range(SETS)]
        hf_lo = [sb(f"hf_lo{s}", [P, C, N], F32R) for s in range(SETS)]
        h_last = [sb(f"h_last{s}", [P, C, N]) for s in range(SETS)]
        a_hi, a_lo = sb("a_hi", [P, C, N], F32R), sb("a_lo", [P, C, N], F32R)
        u_kept = sb("u_kept", [P, C, N])
        r_buf = sb("r_buf", [P, C, N])
        z_buf = sb("z_buf", [P, C, N])
        rh = sb("rh", [P, C, N])
        rh_hi, rh_lo = sb("rh_hi", [P, C, N], F32R), sb("rh_lo", [P, C, N], F32R)
        keep = sb("keep", [P, C, N])
        cand = sb("cand", [P, C, N])
        stats = sb("stats", [P, M, 6])
        mean_var = [sb(f"mean_var{s}", [P, M, 2]) for s in range(SETS)]
        var_eps = sb("var_eps", [P, M])
        minus_half = sb("minus_half", [P, M])
        rstd = [sb(f"rstd{s}", [P, M]) for s in range(SETS)]
        warm = sb("warm", [P, 1])

        bank = [ctx.enter_context(nc.psum_tensor(f"bank{i}", [P, NB], F32)) for i in range(8)]
        turned = bank[0:2]
        agg_z = bank[2:4]
        u_r = bank[4:6]
        cand_ps = bank[6:8]

        ident_zero, ident_ready = sem("ident_zero"), sem("ident_ready")
        half_ready, rows_summed, bias_turned = sem("half_ready"), sem("rows_summed"), sem("bias_turned")
        bias_copied, bias_ready = sem("bias_copied"), sem("bias_ready")
        prep_turned, prep_hi, prep_lo = sem("prep_turned"), sem("prep_hi"), sem("prep_lo")
        mean_ready, stats_ready = sem("mean_ready"), sem("stats_ready")
        eps_added, rstd_ready = sem("eps_added"), sem("rstd_ready")
        normed, h_first_ready = sem("normed"), sem("h_first_ready")
        first_hi, first_lo = sem("first_hi"), sem("first_lo")
        x_copied = sem("x_copied")
        first_turned, h_turned, last_turned = sem("first_turned"), sem("h_turned"), sem("last_turned")
        u_done, agg_done, r_done, z_done, cand_done = (sem(n) for n in ("u_done", "agg_done", "r_done", "z_done", "cand_done"))
        hn_hi_ready, hn_lo_ready = sem("hn_hi_ready"), sem("hn_lo_ready")
        hf_hi_ready, hf_lo_ready = sem("hf_hi_ready"), sem("hf_lo_ready")
        u_copied, a_hi_ready, a_lo_ready = sem("u_copied"), sem("a_hi_ready"), sem("a_lo_ready")
        r_summed, z_summed, r_ready, z_ready = (sem(n) for n in ("r_summed", "z_summed", "r_ready", "z_ready"))
        rh_ready, rh_hi_ready, rh_lo_ready = sem("rh_ready"), sem("rh_hi_ready"), sem("rh_lo_ready")
        keep_ready, cand_ready, zc_ready, h_ready = (sem(n) for n in ("keep_ready", "cand_ready", "zc_ready", "h_ready"))
        out_summed = sem("out_summed")
        pool_passed, dve_passed = sem("pool_passed"), sem("dve_passed")
        adj_loaded = sem("adj_loaded")
        w_loaded = {n: sem(f"{n}_loaded") for n in w_rows}
        bias_loaded = sem("bias_loaded")
        x_loaded = [sem(f"x_loaded{s}") for s in range(SETS)]
        out_stored = [sem(f"out_stored{s}") for s in range(SETS)]

        x_v = x.rearrange("(g s) (p m) d -> g s p m d", s=SETS, m=M)
        out_v = out.rearrange("(g s) (p m) d -> g s p m d", s=SETS, m=M)

        PREP = [("adj", m) for m in range(M)] + [(n, 0) for n in ("u3", "w4", "w3", "w5", "u5")]
        PREP_BANK = [2, 3, 4, 5, 6, 7, 6, 7, 6]
        EARLY = 6
        SUMMED = ["w4", "w3", "w5"]
        BIASES = [u3_b, w4_b, w3_b, w5_b, u5_b]

        def prep_parts(i):
            name, m = PREP[i]
            if name == "adj":
                return adjT_hi[:, m, :], adjT_lo[:, m, :]
            return (wT_hi[name][:, :, :].rearrange("p c d -> p (c d)"),
                    wT_lo[name][:, :, :].rearrange("p c d -> p (c d)"))

        def unit(p, j, c=C - 1):
            return p * (UNITS * C) + (C * j + c + 1)

        def later(p, j, c=C - 1):
            return p * ((UNITS - SETS) * C) + (C * (j - SETS) + c + 1)

        def graph(p, s, c=C - 1):
            return p * (SETS * C) + (C * s + c + 1)

        def once(p, s):
            return p * SETS + (s + 1)

        def after(p, j):
            return (p, j + 1) if j < UNITS - 1 else (p + 1, 0)

        def before(p, j):
            return (p, j - 1) if j else (p - 1, UNITS - 1)

        def pairs(eng, slot):
            slot(0, 0, True, False)
            with eng.Fori(0, PAIRS - 1) as p:
                for j in range(1, UNITS):
                    slot(p, j, False, False)
                slot(p + 1, 0, False, False)
            for j in range(1, UNITS):
                slot(PAIRS - 1, j, False, True)

        def parts_of_bank(t):
            return slice(2 * t, 2 * t + 2)

        block = ctx.enter_context(nc.Block())

        @block.sync
        def _(sp):
            for s in range(SETS):
                sp.dma_start(x_in[s][:, :, :], x_v[0, s]).then_inc(x_loaded[s], 16)
            for n, w in (("u3", u3_w), ("w3", w3_w), ("u5", u5_w)):
                sp.dma_start(w_rows[n][:, :, :], w.rearrange("(c p) i -> p c i", p=P)).then_inc(w_loaded[n], 16)

            def store(p, s):
                sp.wait_ge(out_summed, graph(p, s))
                sp.dma_start(out_v[p, s], x_out[s][:, :, :]).then_inc(out_stored[s], 16)

            with sp.Fori(0, PAIRS - 1) as p:
                for s in range(SETS):
                    sp.wait_ge(x_copied, once(p, s))
                    sp.wait_ge(normed, once(p, s))
                    sp.dma_start(x_in[s][:, :, :], x_v[p + 1, s]).then_inc(x_loaded[s], 16)
                for s in range(SETS):
                    store(p, s)
            for s in range(SETS):
                store(PAIRS - 1, s)
            for s in range(SETS):
                sp.wait_ge(out_stored[s], 16 * PAIRS)

        @block.gpsimd
        def _(pool):
            pool.memset(ident[:, :], 0.0).then_inc(ident_zero, 1)
            pool.memset(minus_half[:, :], -0.5).then_inc(half_ready, 1)
            pool.wait_ge(ident_zero, 1)
            pool.affine_select(out=ident[:, :], in_=ident[:, :], compare_op=ALU.not_equal, fill=1.0, base=0,
                               pattern=[[-1, P]], channel_multiplier=1).then_inc(ident_ready, 1)
            pool.wait_ge(half_ready, 1)

            def inverse_deviation(p, s):
                pool.wait_ge(stats_ready, once(p, s))
                pool.sem_inc(pool_passed, 1)
                pool.tensor_scalar(var_eps[:, :], mean_var[s][:, :, 1], EPS, None, ALU.add).then_inc(eps_added, 1)
                pool.wait_ge(eps_added, once(p, s))
                pool.tensor_tensor(rstd[s][:, :], var_eps[:, :], minus_half[:, :], ALU.pow).then_inc(rstd_ready, 1)

            def keep_x(p, s):
                pool.wait_ge(x_loaded[s], (p + 1) * 16)
                pool.sem_inc(pool_passed, 1)
                pool.tensor_copy(x_out[s][:, :, :], x_in[s][:, :, :]).then_inc(x_copied, 1)

            for s in range(SETS):
                inverse_deviation(0, s)
            for s in range(SETS):
                keep_x(0, s)
            with pool.Fori(0, PAIRS - 1) as p:
                for s in range(SETS):
                    inverse_deviation(p + 1, s)
                for s in range(SETS):
                    pool.wait_ge(out_stored[s], (p + 1) * 16)
                    keep_x(p + 1, s)

        @block.tensor
        def _(pe):
            def products(dst, terms, start=True, stop=True):
                passes = [ab for wh, wl, mh, ml in terms for ab in ((wh, mh), (wh, ml), (wl, mh))]
                for i, (w, m) in enumerate(passes):
                    last = pe.matmul(dst[:, :], w, m, start=start and i == 0, stop=stop and i == len(passes) - 1)
                return last

            def linear(name, dst, c, src_hi, src_lo, **flags):
                return products(dst, [(wT_hi[name][:, i, c * P:(c + 1) * P], wT_lo[name][:, i, c * P:(c + 1) * P],
                                       src_hi[:, i, :], src_lo[:, i, :]) for i in range(C)], **flags)

            def to_nodes(src, dst, t):
                for b in range(2):
                    for c in range(C):
                        m = 2 * t + b
                        last = pe.transpose(dst[:, b * D + c * P:b * D + (c + 1) * P],
                                            src[:, c, m * P:(m + 1) * P], ident[:, :])
                return last

            def turn_first(p, s):
                pe.wait_ge(h_first_ready, once(p, s))
                for c in range(C):
                    for m in range(M):
                        last = pe.transpose(turned[c][:, m * P:(m + 1) * P],
                                            h_first[s][:, m, c * P:(c + 1) * P], ident[:, :])
                    last.then_inc(first_turned, 1)

            def turn_last(p, s, dst):
                pe.wait_ge(h_ready, unit(p, UNITS - SETS + s))
                for t in range(2):
                    to_nodes(h_last[s], dst[t], t).then_inc(last_turned, 1)

            def turn_next(p, j):
                s = j % SETS
                if j < SETS:
                    turn_first(p, s)
                else:
                    pe.wait_ge(h_ready, unit(p, j - SETS))
                    for t in range(2):
                        to_nodes(hf[s], turned[t], t).then_inc(h_turned, 1)

            def prepare(i):
                name, m = PREP[i]
                dst = bank[PREP_BANK[i]]
                if name == "adj":
                    if m == 0:
                        pe.wait_ge(adj_loaded, 16)
                    cols = adj_rows[:, :, :].rearrange("q k (p m) -> q k m p", m=M)
                    for k in range(M):
                        last = pe.transpose(dst[:, k * P:(k + 1) * P], cols[:, k, m, :], ident[:, :])
                else:
                    if name in SUMMED:
                        pe.wait_ge(rows_summed, SUMMED.index(name) + 1)
                    else:
                        pe.wait_ge(w_loaded[name], 16)
                    if i >= EARLY:
                        pe.wait_ge(prep_hi, i - 1)
                        pe.wait_ge(prep_lo, i - 1)
                    for i_c in range(C):
                        for o_c in range(C):
                            last = pe.transpose(dst[:, i_c * D + o_c * P:i_c * D + (o_c + 1) * P],
                                                w_rows[name][:, o_c, i_c * P:(i_c + 1) * P], ident[:, :])
                last.then_inc(prep_turned, 1)

            def u_part(p, j, first):
                s = j % SETS
                pe.wait_ge(hf_hi_ready, unit(p, j))
                pe.wait_ge(hf_lo_ready, unit(p, j))
                if not first:
                    pe.wait_ge(r_summed, unit(*before(p, j)))
                for c in range(C):
                    linear("u3", u_r[c], c, hf_hi[s], hf_lo[s]).then_inc(u_done, 1)

            def aggregate(p, j, first):
                s = j % SETS
                if j < SETS:
                    pe.wait_ge(first_hi, graph(p, s))
                    pe.wait_ge(first_lo, graph(p, s))
                else:
                    pe.wait_ge(hn_hi_ready, later(p, j))
                    pe.wait_ge(hn_lo_ready, later(p, j))
                if not first:
                    pe.wait_ge(z_summed, unit(*before(p, j)))
                for c in range(C):
                    cols = slice(c * P, (c + 1) * P)
                    products(agg_z[c], [(hn_hi[s][:, m, cols], hn_lo[s][:, m, cols],
                                         adjT_hi[:, m, :], adjT_lo[:, m, :]) for m in range(M)]).then_inc(agg_done, 1)

            def candidate_end(p, j):
                for c in range(C):
                    pe.wait_ge(rh_hi_ready, unit(p, j))
                    pe.wait_ge(rh_lo_ready, unit(p, j))
                    linear("u5", cand_ps[c], c, rh_hi, rh_lo, start=False).then_inc(cand_done, 1)

            def slot(p, j, first, last):
                if j < SETS:
                    aggregate(p, j, first)
                    if j == 0 and not first:
                        pe.wait_ge(hf_lo_ready, unit(p, j))
                        turn_last(p - 1, 0, turned)
                    if j == 1:
                        pe.wait_ge(keep_ready, unit(p, 0))
                    u_part(p, j, first)
                else:
                    u_part(p, j, first)
                    aggregate(p, j, first)
                if not first:
                    candidate_end(*before(p, j))
                else:
                    for i in range(EARLY, len(PREP)):
                        prepare(i)
                pe.wait_ge(a_hi_ready, unit(p, j))
                pe.wait_ge(a_lo_ready, unit(p, j))
                pe.wait_ge(u_copied, unit(p, j))
                for c in range(C):
                    linear("w4", u_r[c], c, a_hi, a_lo).then_inc(r_done, 1)
                if first:
                    pe.wait_ge(prep_hi, len(PREP))
                    pe.wait_ge(prep_lo, len(PREP))
                for c in range(C):
                    linear("w3", agg_z[c], c, a_hi, a_lo).then_inc(z_done, 1)
                if j == 0 and not first:
                    pe.wait_ge(out_summed, graph(p - 1, 0))
                if not (last and j == UNITS - 1):
                    turn_next(*after(p, j))
                if not first:
                    pe.wait_ge(cand_ready, unit(*before(p, j)))
                for c in range(C):
                    linear("w5", cand_ps[c], c, a_hi, a_lo, stop=False)
                if j == 0 and not first:
                    pe.wait_ge(r_summed, unit(p, j))
                    turn_last(p - 1, 1, u_r)

            pe.wait_ge(ident_ready, 1)
            turn_first(0, 0)
            for i in range(M):
                prepare(i)
            pe.wait_ge(bias_loaded, 16 * len(BIASES))
            pe.transpose(bank[7][:, 0:5 * C], bias_rows[:, :], ident[0:5 * C, 0:5 * C]).then_inc(bias_turned, 1)
            prepare(M)
            pe.wait_ge(bias_copied, 1)
            prepare(M + 1)
            pe.wait_ge(prep_hi, EARLY)
            pe.wait_ge(prep_lo, EARLY)
            pairs(pe, slot)
            candidate_end(PAIRS - 1, UNITS - 1)
            pe.wait_ge(r_summed, unit(PAIRS - 1, UNITS - 1))
            for s in range(SETS):
                turn_last(PAIRS - 1, s, (turned, u_r)[s])

        @block.scalar
        def _(act):
            act.dma_start(adj_rows[:, :, :], adj.rearrange("(q k) n -> q k n", k=M)).then_inc(adj_loaded, 16)
            for i, b in enumerate(BIASES):
                act.dma_start(bias_rows[C * i:C * (i + 1), :], b.rearrange("(c p) -> c p", p=P)).then_inc(bias_loaded, 16)
            for n, w in (("w4", w4_w), ("w5", w5_w)):
                act.dma_start(w_rows[n][:, :, :], w.rearrange("(c p) i -> p c i", p=P)).then_inc(w_loaded[n], 16)
            act.wait_ge(half_ready, 1)
            act.activation(warm[:, :], minus_half[:, 0:1], ACT.Sigmoid)

            def copy(dst, src):
                return act.activation(dst, src, ACT.Copy)

            def split_first(p, s):
                act.wait_ge(h_first_ready, once(p, s))
                for t in range(2):
                    b = parts_of_bank(t)
                    copy(hn_hi[s][:, b, :], h_first[s][:, b, :]).then_inc(first_hi, 1)

            def take_first(p, s):
                for c in range(C):
                    act.wait_ge(first_turned, graph(p, s, c))
                    copy(hf[s][:, c, :], turned[c][:, :])
                    copy(hf_hi[s][:, c, :], turned[c][:, :]).then_inc(hf_hi_ready, 1)

            def take_next(p, j):
                s = j % SETS
                if j < SETS:
                    take_first(p, s)
                else:
                    for t in range(2):
                        act.wait_ge(h_turned, later(p, j, t))
                        copy(hn_hi[s][:, parts_of_bank(t), :], turned[t][:, :]).then_inc(hn_hi_ready, 1)

            def prepare(i):
                act.wait_ge(prep_turned, i + 1)
                copy(prep_parts(i)[0], bank[PREP_BANK[i]][:, :]).then_inc(prep_hi, 1)

            def slot(p, j, first, last):
                s = j % SETS
                def keep_u():
                    for c in range(C):
                        act.wait_ge(u_done, unit(p, j, c))
                        copy(u_kept[:, c, :], u_r[c][:, :]).then_inc(u_copied, 1)

                if j >= SETS:
                    keep_u()
                for c in range(C):
                    act.wait_ge(agg_done, unit(p, j, c))
                    copy(a_hi[:, c, :], agg_z[c][:, :]).then_inc(a_hi_ready, 1)
                if j < SETS:
                    keep_u()
                if first:
                    for i in range(EARLY, len(PREP)):
                        prepare(i)
                if not first:
                    candidate(*before(p, j))
                for c in range(C):
                    act.wait_ge(r_summed, unit(p, j, c))
                    act.activation(r_buf[:, c, :], r_buf[:, c, :], ACT.Sigmoid,
                                   bias=gate_bias[:, 0, c:c + 1]).then_inc(r_ready, 1)
                    if not first and before(p, j)[1] < UNITS - SETS:
                        q = before(p, j)
                        act.wait_ge(h_ready, unit(*q, c))
                        copy(hf_hi[1 - s][:, c, :], hf[1 - s][:, c, :]).then_inc(hf_hi_ready, 1)
                for c in range(C):
                    act.wait_ge(rh_ready, unit(p, j, c))
                    copy(rh_hi[:, c, :], rh[:, c, :]).then_inc(rh_hi_ready, 1)
                if not (last and j == UNITS - 1):
                    take_next(*after(p, j))
                for c in range(C):
                    act.wait_ge(z_summed, unit(p, j, c))
                    act.activation(z_buf[:, c, :], z_buf[:, c, :], ACT.Sigmoid,
                                   bias=gate_bias[:, 1, c:c + 1]).then_inc(z_ready, 1)
                if not last and j >= UNITS - SETS:
                    split_first(p + 1, s)

            def candidate(p, j):
                for c in range(C):
                    act.wait_ge(cand_done, unit(p, j, c))
                    act.activation(cand[:, c, :], cand_ps[c][:, :], ACT.Tanh,
                                   bias=gate_bias[:, 2, c:c + 1]).then_inc(cand_ready, 1)

            split_first(0, 0)
            take_first(0, 0)
            for i in range(M):
                prepare(i)
            act.wait_ge(bias_turned, 1)
            copy(bias_cols[:, :, :], bank[7][:, 0:5 * C].rearrange("p (b c) -> p b c", c=C)).then_inc(bias_copied, 1)
            for i in range(M, EARLY):
                prepare(i)
            split_first(0, 1)
            act.wait_ge(bias_ready, 3)
            pairs(act, slot)
            candidate(PAIRS - 1, UNITS - 1)

        @block.vector
        def _(dve):
            def f32(ap):
                return ap.bitcast(F32)

            def low(dst, src, hi):
                return dve.tensor_tensor(dst, src, f32(hi), ALU.subtract)

            def statistics(p, s):
                dve.wait_ge(x_loaded[s], (p + 1) * 16)
                for m in range(M):
                    last = dve.bn_stats(stats[:, m, :], x_in[s][:, m, :])
                last.then_inc(mean_ready, 1)
                dve.wait_ge(mean_ready, once(p, s))
                dve.sem_inc(dve_passed, 1)
                for m in range(M):
                    last = dve.bn_aggr(mean_var[s][:, m, :], stats[:, m, :])
                last.then_inc(stats_ready, 1)

            def normalise(p, s):
                dve.wait_ge(rstd_ready, once(p, s))
                for m in range(M):
                    last = dve.tensor_scalar(h_first[s][:, m, :], x_in[s][:, m, :], mean_var[s][:, m, 0:1],
                                             rstd[s][:, m:m + 1], ALU.subtract, ALU.mult)
                last.then_inc(normed, 1)
                dve.wait_ge(normed, once(p, s))
                dve.tensor_scalar(h_first[s][:, :, :], h_first[s][:, :, :], 0.0, None, ALU.max).then_inc(h_first_ready, 1)

            def split_first(p, s):
                for t in range(2):
                    b = parts_of_bank(t)
                    dve.wait_ge(first_hi, graph(p, s, t))
                    low(hn_lo[s][:, b, :], h_first[s][:, b, :], hn_hi[s][:, b, :]).then_inc(first_lo, 1)

            def take_first(p, s):
                for c in range(C):
                    dve.wait_ge(hf_hi_ready, unit(p, s, c))
                    low(hf_lo[s][:, c, :], turned[c][:, :], hf_hi[s][:, c, :]).then_inc(hf_lo_ready, 1)

            def prepare(i):
                dve.wait_ge(prep_hi, i + 1)
                hi, lo = prep_parts(i)
                low(lo, bank[PREP_BANK[i]][:, :], hi).then_inc(prep_lo, 1)

            def take_next(p, j):
                s = j % SETS
                if j < SETS:
                    take_first(p, s)
                else:
                    for t in range(2):
                        b = parts_of_bank(t)
                        dve.wait_ge(hn_hi_ready, later(p, j, t))
                        low(hn_lo[s][:, b, :], turned[t][:, :].rearrange("p (b d) -> p b d", d=D),
                            hn_hi[s][:, b, :]).then_inc(hn_lo_ready, 1)

            def add_x(p, s):
                src = (turned, u_r)[s]
                dve.wait_ge(x_copied, once(p, s))
                for t in range(2):
                    b = parts_of_bank(t)
                    dve.wait_ge(last_turned, graph(p, s, t))
                    dve.tensor_tensor(x_out[s][:, b, :], src[t][:, :].rearrange("p (b d) -> p b d", d=D),
                                      x_out[s][:, b, :], ALU.add).then_inc(out_summed, 1)

            def new_h(p, j, c):
                s = j % SETS
                dve.wait_ge(cand_ready, unit(p, j, c))
                dve.tensor_tensor(cand[:, c, :], z_buf[:, c, :], cand[:, c, :], ALU.mult).then_inc(zc_ready, 1)
                dve.wait_ge(zc_ready, unit(p, j, c))
                dst = h_last[s] if j >= UNITS - SETS else hf[s]
                dve.tensor_tensor(dst[:, c, :], cand[:, c, :], keep[:, c, :], ALU.subtract).then_inc(h_ready, 1)

            def slot(p, j, first, last):
                s = j % SETS
                for c in range(C):
                    dve.wait_ge(a_hi_ready, unit(p, j, c))
                    low(a_lo[:, c, :], agg_z[c][:, :], a_hi[:, c, :]).then_inc(a_lo_ready, 1)
                if j == 0 and not first:
                    add_x(p - 1, 0)
                if first:
                    for i in range(EARLY, len(PREP)):
                        prepare(i)
                for c in range(C):
                    if not first:
                        new_h(*before(p, j), c)
                    dve.wait_ge(u_copied, unit(p, j, c))
                    dve.wait_ge(r_done, unit(p, j, c))
                    dve.tensor_tensor(r_buf[:, c, :], u_r[c][:, :], u_kept[:, c, :], ALU.add).then_inc(r_summed, 1)
                for c in range(C):
                    dve.wait_ge(r_ready, unit(p, j, c))
                    dve.tensor_tensor(rh[:, c, :], r_buf[:, c, :], hf[s][:, c, :], ALU.mult).then_inc(rh_ready, 1)
                if not first and before(p, j)[1] < UNITS - SETS:
                    q = before(p, j)
                    for c in range(C):
                        dve.wait_ge(hf_hi_ready, unit(q[0], q[1] + SETS, c))
                        low(hf_lo[1 - s][:, c, :], hf[1 - s][:, c, :], hf_hi[1 - s][:, c, :]).then_inc(hf_lo_ready, 1)
                for c in range(C):
                    dve.wait_ge(rh_hi_ready, unit(p, j, c))
                    low(rh_lo[:, c, :], rh[:, c, :], rh_hi[:, c, :]).then_inc(rh_lo_ready, 1)
                for c in range(C):
                    dve.wait_ge(z_done, unit(p, j, c))
                    dve.tensor_tensor(z_buf[:, c, :], agg_z[c][:, :], u_kept[:, c, :], ALU.add).then_inc(z_summed, 1)
                if not (last and j == UNITS - 1):
                    take_next(*after(p, j))
                if j == 0 and not first:
                    add_x(p - 1, 1)
                for c in range(C):
                    dve.wait_ge(z_ready, unit(p, j, c))
                    dve.scalar_tensor_tensor(out=keep[:, c, :], in0=z_buf[:, c, :], scalar=1.0, in1=hf[s][:, c, :],
                                             op0=ALU.subtract, op1=ALU.mult).then_inc(keep_ready, 1)
                if not last and j >= UNITS - SETS:
                    normalise(p + 1, s)
                    split_first(p + 1, s)
                if not last and j in (UNITS - SETS - 1, UNITS - SETS):
                    statistics(p + 1, j - (UNITS - SETS - 1))

            statistics(0, 0)
            normalise(0, 0)
            split_first(0, 0)
            take_first(0, 0)
            statistics(0, 1)
            for i in range(M):
                prepare(i)
            for k, n in enumerate(SUMMED):
                dve.wait_ge(w_loaded[n], 16)
                dve.tensor_tensor(w_rows[n][:, :, 0:D], w_rows[n][:, :, 0:D], w_rows[n][:, :, D:2 * D],
                                  ALU.add).then_inc(rows_summed, 1)
                if k == 0:
                    for i in range(M, EARLY):
                        prepare(i)
                    normalise(0, 1)
                    split_first(0, 1)
            dve.wait_ge(bias_copied, 1)
            for g, (b0, b1) in enumerate(((1, 0), (2, 0), (3, 4))):
                dve.tensor_tensor(gate_bias[:, g, :], bias_cols[:, b0, :], bias_cols[:, b1, :],
                                  ALU.add).then_inc(bias_ready, 1)
            pairs(dve, slot)
            for c in range(C):
                new_h(PAIRS - 1, UNITS - 1, c)
            for s in range(SETS):
                add_x(PAIRS - 1, s)


_INS = ["x", "adj", "L0_gnn_w3_w", "L0_gnn_w3_b", "L0_gnn_u3_w", "L0_gnn_u3_b", "L0_gnn_w4_w", "L0_gnn_w4_b",
        "L0_gnn_w5_w", "L0_gnn_w5_b", "L0_gnn_u5_w", "L0_gnn_u5_b"]


def kernel(**inputs):
    import numpy as np
    import concourse.bacc as bacc
    from concourse.bass_utils import run_bass_kernel_spmd

    nc = bacc.Bacc("TRN2", target_bir_lowering=False, num_devices=1)
    arrays, args = {}, []
    for name in _INS:
        a = np.ascontiguousarray(inputs[name])
        arrays[f"in_{name}"] = a
        args.append(nc.dram_tensor(f"in_{name}", a.shape, mybir.dt.from_np(a.dtype), kind="ExternalInput").ap())
    out = nc.dram_tensor("out", inputs["x"].shape, F32, kind="ExternalOutput").ap()
    gated_graph_network(nc, *args, out)
    result = run_bass_kernel_spmd(nc, [arrays], core_ids=[0])
    return result.results[0]["out"]
```

```python
from contextlib import ExitStack

from concourse import mybir

F32 = mybir.dt.float32
F32R = mybir.dt.float32r
ALU = mybir.AluOpType
ACT = mybir.ActivationFunctionType

P = 128
NB = 512
STEPS = 3
SETS = 2
UNITS = STEPS * SETS
EPS = 1e-5


def gated_graph_network(nc, x, adj, w3_w, w3_b, u3_w, u3_b, w4_w, w4_b, w5_w, w5_b, u5_w, u5_b, out):
    B, N, D = x.shape
    M = N // P
    C = D // P
    PAIRS = B // SETS

    ctx = ExitStack()
    with ctx:
        def sb(name, shape, dt=F32):
            return ctx.enter_context(nc.sbuf_tensor(name, shape, dt))

        def sem(name):
            return ctx.enter_context(nc.semaphore(name))

        ident = sb("ident", [P, P])
        adj_rows = sb("adj_rows", [P, M, N])
        adjT_hi, adjT_lo = sb("adjT_hi", [P, M, N], F32R), sb("adjT_lo", [P, M, N], F32R)
        w_rows = {n: sb(f"{n}_rows", [P, C, 2 * D]) for n in ("w4", "w3", "w5")}
        w_rows |= {n: sb(f"{n}_rows", [P, C, D]) for n in ("u3", "u5")}
        wT_hi = {n: sb(f"{n}T_hi", [P, C, D], F32R) for n in w_rows}
        wT_lo = {n: sb(f"{n}T_lo", [P, C, D], F32R) for n in w_rows}
        bias_rows = sb("bias_rows", [5 * C, P])
        bias_cols = sb("bias_cols", [P, 5, C])
        gate_bias = sb("gate_bias", [P, 3, C])
        x_in = [sb(f"x_in{s}", [P, M, D]) for s in range(SETS)]
        x_out = [sb(f"x_out{s}", [P, M, D]) for s in range(SETS)]
        h_first = [sb(f"h_first{s}", [P, M, D]) for s in range(SETS)]
        hn_hi = [sb(f"hn_hi{s}", [P, M, D], F32R) for s in range(SETS)]
        hn_lo = [sb(f"hn_lo{s}", [P, M, D], F32R) for s in range(SETS)]
        hf = [sb(f"hf{s}", [P, C, N]) for s in range(SETS)]
        hf_hi = [sb(f"hf_hi{s}", [P, C, N], F32R) for s in range(SETS)]
        hf_lo = [sb(f"hf_lo{s}", [P, C, N], F32R) for s in range(SETS)]
        h_last = [sb(f"h_last{s}", [P, C, N]) for s in range(SETS)]
        a_hi, a_lo = sb("a_hi", [P, C, N], F32R), sb("a_lo", [P, C, N], F32R)
        u_kept = sb("u_kept", [P, C, N])
        r_buf = sb("r_buf", [P, C, N])
        z_buf = sb("z_buf", [P, C, N])
        rh = sb("rh", [P, C, N])
        rh_hi, rh_lo = sb("rh_hi", [P, C, N], F32R), sb("rh_lo", [P, C, N], F32R)
        keep = sb("keep", [P, C, N])
        cand = sb("cand", [P, C, N])
        stats = sb("stats", [P, M, 6])
        mean_var = [sb(f"mean_var{s}", [P, M, 2]) for s in range(SETS)]
        var_eps = sb("var_eps", [P, M])
        minus_half = sb("minus_half", [P, M])
        rstd = [sb(f"rstd{s}", [P, M]) for s in range(SETS)]
        warm = sb("warm", [P, 1])

        bank = [ctx.enter_context(nc.psum_tensor(f"bank{i}", [P, NB], F32)) for i in range(8)]
        turned = bank[0:2]
        agg_z = bank[2:4]
        u_r = bank[4:6]
        cand_ps = bank[6:8]

        ident_zero, ident_ready = sem("ident_zero"), sem("ident_ready")
        half_ready, rows_summed, bias_turned = sem("half_ready"), sem("rows_summed"), sem("bias_turned")
        bias_copied, bias_ready = sem("bias_copied"), sem("bias_ready")
        prep_turned, prep_hi, prep_lo = sem("prep_turned"), sem("prep_hi"), sem("prep_lo")
        mean_ready, stats_ready = sem("mean_ready"), sem("stats_ready")
        eps_added, rstd_ready = sem("eps_added"), sem("rstd_ready")
        normed, h_first_ready = sem("normed"), sem("h_first_ready")
        first_hi, first_lo = sem("first_hi"), sem("first_lo")
        first_turned, h_turned, last_turned = sem("first_turned"), sem("h_turned"), sem("last_turned")
        u_done, agg_done, r_done, z_done, cand_done = (sem(n) for n in ("u_done", "agg_done", "r_done", "z_done", "cand_done"))
        hn_hi_ready, hn_lo_ready = sem("hn_hi_ready"), sem("hn_lo_ready")
        hf_hi_ready, hf_lo_ready = sem("hf_hi_ready"), sem("hf_lo_ready")
        u_copied, a_hi_ready, a_lo_ready = sem("u_copied"), sem("a_hi_ready"), sem("a_lo_ready")
        r_summed, z_summed, r_ready, z_ready = (sem(n) for n in ("r_summed", "z_summed", "r_ready", "z_ready"))
        rh_ready, rh_hi_ready, rh_lo_ready = sem("rh_ready"), sem("rh_hi_ready"), sem("rh_lo_ready")
        keep_ready, cand_ready, zc_ready, h_ready = (sem(n) for n in ("keep_ready", "cand_ready", "zc_ready", "h_ready"))
        out_summed = sem("out_summed")
        pool_passed, dve_passed, sp_passed = sem("pool_passed"), sem("dve_passed"), sem("sp_passed")
        adj_loaded = sem("adj_loaded")
        w_loaded = {n: sem(f"{n}_loaded") for n in w_rows}
        bias_loaded = sem("bias_loaded")
        x_copied = [sem(f"x_copied{s}") for s in range(SETS)]
        x_loaded = [sem(f"x_loaded{s}") for s in range(SETS)]
        out_stored = [sem(f"out_stored{s}") for s in range(SETS)]

        x_v = x.rearrange("(g s) (p m) d -> g s p m d", s=SETS, m=M)
        out_v = out.rearrange("(g s) (p m) d -> g s p m d", s=SETS, m=M)

        PREP = [("adj", m) for m in range(M)] + [(n, 0) for n in ("u3", "w4", "w3", "w5", "u5")]
        PREP_BANK = [2, 3, 4, 5, 6, 7, 6, 7, 6]
        EARLY = M + 2
        SUMMED = ["w4", "w3", "w5"]
        BIASES = [u3_b, w4_b, w3_b, w5_b, u5_b]

        def prep_parts(i):
            name, m = PREP[i]
            if name == "adj":
                return adjT_hi[:, m, :], adjT_lo[:, m, :]
            return (wT_hi[name][:, :, :].rearrange("p c d -> p (c d)"),
                    wT_lo[name][:, :, :].rearrange("p c d -> p (c d)"))

        def unit(p, j, c=C - 1):
            return p * (UNITS * C) + (C * j + c + 1)

        def later(p, j, c=C - 1):
            return p * ((UNITS - SETS) * C) + (C * (j - SETS) + c + 1)

        def graph(p, s, c=C - 1):
            return p * (SETS * C) + (C * s + c + 1)

        def once(p, s):
            return p * SETS + (s + 1)

        def after(p, j):
            return (p, j + 1) if j < UNITS - 1 else (p + 1, 0)

        def before(p, j):
            return (p, j - 1) if j else (p - 1, UNITS - 1)

        def pairs(eng, slot):
            slot(0, 0, True, False)
            with eng.Fori(0, PAIRS - 1) as p:
                for j in range(1, UNITS):
                    slot(p, j, False, False)
                slot(p + 1, 0, False, False)
            for j in range(1, UNITS):
                slot(PAIRS - 1, j, False, True)

        def parts_of_bank(t):
            return slice(2 * t, 2 * t + 2)

        block = ctx.enter_context(nc.Block())

        @block.sync
        def _(sp):
            def load_weight(name, w):
                sp.dma_start(w_rows[name][:, :, :], w.rearrange("(c p) i -> p c i", p=P)).then_inc(w_loaded[name], 16)

            def load_x(p, s):
                sp.dma_start(x_in[s][:, :, :], x_v[p, s]).then_inc(x_loaded[s], 16)

            def keep_x(p, s):
                sp.wait_ge(x_loaded[s], 16 * (p + 1))
                sp.dma_start(x_out[s][:, :, :], x_in[s][:, :, :]).then_inc(x_copied[s], 16)

            def next_x(p, s):
                sp.wait_ge(x_copied[s], 16 * p)
                sp.sem_inc(sp_passed, 1)
                sp.wait_ge(normed, once(p - 1, s))
                sp.sem_inc(sp_passed, 1)
                load_x(p, s)

            def store(p, s):
                sp.wait_ge(out_summed, graph(p, s))
                sp.sem_inc(sp_passed, 1)
                sp.dma_start(out_v[p, s], x_out[s][:, :, :]).then_inc(out_stored[s], 16)

            def store_and_refill(p, s):
                store(p, s)
                sp.wait_ge(out_stored[s], 16 * (p + 1))
                sp.sem_inc(sp_passed, 1)
                keep_x(p + 1, s)

            load_x(0, 0)
            load_weight("u3", u3_w)
            load_weight("w3", w3_w)
            load_x(0, 1)
            load_weight("u5", u5_w)
            for s in range(SETS):
                keep_x(0, s)
            for s in range(SETS):
                next_x(1, s)
            with sp.Fori(0, PAIRS - 2) as p:
                for s in range(SETS):
                    store_and_refill(p, s)
                for s in range(SETS):
                    next_x(p + 2, s)
            for s in range(SETS):
                store_and_refill(PAIRS - 2, s)
            for s in range(SETS):
                for t in range(2):
                    sp.wait_ge(out_summed, graph(PAIRS - 1, s, t))
                    b = parts_of_bank(t)
                    sp.dma_start(out_v[PAIRS - 1, s][:, b, :], x_out[s][:, b, :]).then_inc(out_stored[s], 16)
            for s in range(SETS):
                sp.wait_ge(out_stored[s], 16 * (PAIRS + 1))

        @block.gpsimd
        def _(pool):
            pool.memset(ident[:, :], 0.0).then_inc(ident_zero, 1)
            pool.memset(minus_half[:, :], -0.5).then_inc(half_ready, 1)
            pool.wait_ge(ident_zero, 1)
            pool.affine_select(out=ident[:, :], in_=ident[:, :], compare_op=ALU.not_equal, fill=1.0, base=0,
                               pattern=[[-1, P]], channel_multiplier=1).then_inc(ident_ready, 1)
            pool.wait_ge(half_ready, 1)

            def inverse_deviation(p, s):
                pool.wait_ge(stats_ready, once(p, s))
                pool.sem_inc(pool_passed, 1)
                pool.tensor_scalar(var_eps[:, :], mean_var[s][:, :, 1], EPS, None, ALU.add).then_inc(eps_added, 1)
                pool.wait_ge(eps_added, once(p, s))
                pool.tensor_tensor(rstd[s][:, :], var_eps[:, :], minus_half[:, :], ALU.pow).then_inc(rstd_ready, 1)

            def sum_halves(name):
                pool.wait_ge(w_loaded[name], 16)
                pool.tensor_tensor(w_rows[name][:, :, 0:D], w_rows[name][:, :, 0:D], w_rows[name][:, :, D:2 * D],
                                   ALU.add).then_inc(rows_summed, 1)

            inverse_deviation(0, 0)
            sum_halves("w4")
            sum_halves("w3")
            inverse_deviation(0, 1)
            sum_halves("w5")
            with pool.Fori(0, PAIRS - 1) as p:
                for s in range(SETS):
                    inverse_deviation(p + 1, s)

        @block.tensor
        def _(pe):
            def products(dst, terms, start=True, stop=True):
                passes = [ab for wh, wl, mh, ml in terms for ab in ((wh, mh), (wh, ml), (wl, mh))]
                for i, (w, m) in enumerate(passes):
                    last = pe.matmul(dst[:, :], w, m, start=start and i == 0, stop=stop and i == len(passes) - 1)
                return last

            def linear(name, dst, c, src_hi, src_lo, blocks=range(C), **flags):
                return products(dst, [(wT_hi[name][:, i, c * P:(c + 1) * P], wT_lo[name][:, i, c * P:(c + 1) * P],
                                       src_hi[:, i, :], src_lo[:, i, :]) for i in blocks], **flags)

            def to_nodes(src, dst, t):
                for b in range(2):
                    for c in range(C):
                        m = 2 * t + b
                        last = pe.transpose(dst[:, b * D + c * P:b * D + (c + 1) * P],
                                            src[:, c, m * P:(m + 1) * P], ident[:, :])
                return last

            def turn_first(p, s):
                pe.wait_ge(h_first_ready, once(p, s))
                for c in range(C):
                    for m in range(M):
                        last = pe.transpose(turned[c][:, m * P:(m + 1) * P],
                                            h_first[s][:, m, c * P:(c + 1) * P], ident[:, :])
                    last.then_inc(first_turned, 1)

            def turn_last(p, s, dst):
                pe.wait_ge(h_ready, unit(p, UNITS - SETS + s))
                for t in range(2):
                    to_nodes(h_last[s], dst[t], t).then_inc(last_turned, 1)

            def turn_next(p, j):
                s = j % SETS
                if j < SETS:
                    turn_first(p, s)
                else:
                    pe.wait_ge(h_ready, unit(p, j - SETS))
                    for t in range(2):
                        to_nodes(hf[s], turned[t], t).then_inc(h_turned, 1)

            def prepare(i):
                name, m = PREP[i]
                dst = bank[PREP_BANK[i]]
                if name == "adj":
                    if m == 0:
                        pe.wait_ge(adj_loaded, 16)
                    cols = adj_rows[:, :, :].rearrange("q k (p m) -> q k m p", m=M)
                    for k in range(M):
                        last = pe.transpose(dst[:, k * P:(k + 1) * P], cols[:, k, m, :], ident[:, :])
                else:
                    if name in SUMMED:
                        pe.wait_ge(rows_summed, SUMMED.index(name) + 1)
                    else:
                        pe.wait_ge(w_loaded[name], 16)
                    if i >= EARLY:
                        pe.wait_ge(prep_hi, i - 1)
                        pe.wait_ge(prep_lo, i - 1)
                    for i_c in range(C):
                        for o_c in range(C):
                            last = pe.transpose(dst[:, i_c * D + o_c * P:i_c * D + (o_c + 1) * P],
                                                w_rows[name][:, o_c, i_c * P:(i_c + 1) * P], ident[:, :])
                last.then_inc(prep_turned, 1)

            def u_part(p, j, first):
                s = j % SETS
                pe.wait_ge(hf_hi_ready, unit(p, j))
                pe.wait_ge(hf_lo_ready, unit(p, j))
                if not first:
                    pe.wait_ge(r_summed, unit(*before(p, j)))
                for c in range(C):
                    linear("u3", u_r[c], c, hf_hi[s], hf_lo[s]).then_inc(u_done, 1)

            def aggregate(p, j, first):
                s = j % SETS
                if j < SETS:
                    pe.wait_ge(first_hi, graph(p, s))
                    pe.wait_ge(first_lo, graph(p, s))
                else:
                    pe.wait_ge(hn_hi_ready, later(p, j))
                    pe.wait_ge(hn_lo_ready, later(p, j))
                if not first:
                    pe.wait_ge(z_summed, unit(*before(p, j)))
                for c in range(C):
                    cols = slice(c * P, (c + 1) * P)
                    for m in range(M):
                        if first:
                            pe.wait_ge(prep_hi, max(m, c) + 1)
                            pe.wait_ge(prep_lo, max(m, c) + 1)
                        done = products(agg_z[c], [(hn_hi[s][:, m, cols], hn_lo[s][:, m, cols],
                                                    adjT_hi[:, m, :], adjT_lo[:, m, :])],
                                        start=m == 0, stop=m == M - 1)
                    done.then_inc(agg_done, 1)
                    if first and c == 0:
                        for i in range(M, EARLY):
                            prepare(i)

            def candidate_end(p, j):
                pe.wait_ge(rh_hi_ready, unit(p, j))
                pe.wait_ge(rh_lo_ready, unit(p, j))
                for c in range(C):
                    linear("u5", cand_ps[c], c, rh_hi, rh_lo, start=False).then_inc(cand_done, 1)

            def slot(p, j, first, last):
                if j < SETS:
                    aggregate(p, j, first)
                    if first:
                        pe.wait_ge(prep_hi, M + 1)
                        pe.wait_ge(prep_lo, M + 1)
                    if j == 0 and not first:
                        pe.wait_ge(hf_lo_ready, unit(p, j))
                        turn_last(p - 1, 0, turned)
                    if j == 1:
                        pe.wait_ge(keep_ready, unit(p, 0))
                    u_part(p, j, first)
                else:
                    u_part(p, j, first)
                    aggregate(p, j, first)
                if not first:
                    candidate_end(*before(p, j))
                else:
                    for i in range(EARLY, len(PREP) - 1):
                        prepare(i)
                    pe.wait_ge(bias_loaded, 16 * len(BIASES))
                    pe.transpose(turned[0][:, 0:5 * C], bias_rows[:, :],
                                 ident[0:5 * C, 0:5 * C]).then_inc(bias_turned, 1)
                pe.wait_ge(u_copied, unit(p, j))
                if first:
                    pe.wait_ge(prep_hi, EARLY)
                    pe.wait_ge(prep_lo, EARLY)
                for i in range(C):
                    pe.wait_ge(a_hi_ready, unit(p, j, i))
                    pe.wait_ge(a_lo_ready, unit(p, j, i))
                    for c in range(C):
                        done = linear("w4", u_r[c], c, a_hi, a_lo, blocks=[i], start=i == 0, stop=i == C - 1)
                        if i == C - 1:
                            done.then_inc(r_done, 1)
                if first:
                    prepare(len(PREP) - 1)
                    pe.wait_ge(bias_copied, 1)
                    pe.wait_ge(prep_hi, EARLY + 1)
                    pe.wait_ge(prep_lo, EARLY + 1)
                for c in range(C):
                    linear("w3", agg_z[c], c, a_hi, a_lo).then_inc(z_done, 1)
                if j == 0 and not first:
                    pe.wait_ge(out_summed, graph(p - 1, 0))
                if not (last and j == UNITS - 1):
                    turn_next(*after(p, j))
                if first:
                    pe.wait_ge(prep_hi, len(PREP))
                    pe.wait_ge(prep_lo, len(PREP))
                else:
                    pe.wait_ge(cand_ready, unit(*before(p, j)))
                for c in range(C):
                    linear("w5", cand_ps[c], c, a_hi, a_lo, stop=False)
                if j == 0 and not first:
                    pe.wait_ge(r_summed, unit(p, j))
                    turn_last(p - 1, 1, u_r)

            pe.wait_ge(ident_ready, 1)
            for m in range(M):
                prepare(m)
            turn_first(0, 0)
            pairs(pe, slot)
            pe.wait_ge(hn_lo_ready, later(PAIRS - 1, UNITS - 1))
            turn_last(PAIRS - 1, 0, turned)
            candidate_end(PAIRS - 1, UNITS - 1)
            pe.wait_ge(r_summed, unit(PAIRS - 1, UNITS - 1))
            turn_last(PAIRS - 1, 1, u_r)

        @block.scalar
        def _(act):
            act.dma_start(adj_rows[:, :, :], adj.rearrange("(q k) n -> q k n", k=M)).then_inc(adj_loaded, 16)
            for n, w in (("w4", w4_w), ("w5", w5_w)):
                act.dma_start(w_rows[n][:, :, :], w.rearrange("(c p) i -> p c i", p=P)).then_inc(w_loaded[n], 16)
            for i, b in enumerate(BIASES):
                act.dma_start(bias_rows[C * i:C * (i + 1), :], b.rearrange("(c p) -> c p", p=P)).then_inc(bias_loaded, 16)
            act.wait_ge(half_ready, 1)
            act.activation(warm[:, :], minus_half[:, 0:1], ACT.Sigmoid)

            def copy(dst, src):
                return act.activation(dst, src, ACT.Copy)

            def split_first(p, s):
                act.wait_ge(h_first_ready, once(p, s))
                for t in range(2):
                    b = parts_of_bank(t)
                    copy(hn_hi[s][:, b, :], h_first[s][:, b, :]).then_inc(first_hi, 1)

            def take_first(p, s):
                for c in range(C):
                    act.wait_ge(first_turned, graph(p, s, c))
                    copy(hf[s][:, c, :], turned[c][:, :])
                    copy(hf_hi[s][:, c, :], turned[c][:, :]).then_inc(hf_hi_ready, 1)

            def take_next(p, j):
                s = j % SETS
                if j < SETS:
                    take_first(p, s)
                else:
                    for t in range(2):
                        act.wait_ge(h_turned, later(p, j, t))
                        copy(hn_hi[s][:, parts_of_bank(t), :], turned[t][:, :]).then_inc(hn_hi_ready, 1)

            def prepare(i):
                act.wait_ge(prep_turned, i + 1)
                copy(prep_parts(i)[0], bank[PREP_BANK[i]][:, :]).then_inc(prep_hi, 1)

            def slot(p, j, first, last):
                s = j % SETS

                def keep_u():
                    for c in range(C):
                        act.wait_ge(u_done, unit(p, j, c))
                        copy(u_kept[:, c, :], u_r[c][:, :]).then_inc(u_copied, 1)

                if j >= SETS:
                    keep_u()
                for c in range(C):
                    act.wait_ge(agg_done, unit(p, j, c))
                    copy(a_hi[:, c, :], agg_z[c][:, :]).then_inc(a_hi_ready, 1)
                if j < SETS:
                    keep_u()
                if first:
                    split_first(0, 1)
                    for i in range(EARLY, len(PREP) - 1):
                        prepare(i)
                    act.wait_ge(bias_turned, 1)
                    copy(bias_cols[:, :, :],
                         turned[0][:, 0:5 * C].rearrange("p (b c) -> p b c", c=C)).then_inc(bias_copied, 1)
                    prepare(len(PREP) - 1)
                    act.wait_ge(bias_ready, 3)
                else:
                    candidate(*before(p, j))
                for c in range(C):
                    if not first and before(p, j)[1] < UNITS - SETS:
                        act.wait_ge(h_ready, unit(*before(p, j), c))
                        copy(hf_hi[1 - s][:, c, :], hf[1 - s][:, c, :]).then_inc(hf_hi_ready, 1)
                    act.wait_ge(r_summed, unit(p, j, c))
                    act.activation(r_buf[:, c, :], r_buf[:, c, :], ACT.Sigmoid,
                                   bias=gate_bias[:, 0, c:c + 1]).then_inc(r_ready, 1)
                if not (last and j == UNITS - 1):
                    take_next(*after(p, j))
                for c in range(C):
                    act.wait_ge(rh_ready, unit(p, j, c))
                    copy(rh_hi[:, c, :], rh[:, c, :]).then_inc(rh_hi_ready, 1)
                for c in range(C):
                    act.wait_ge(z_summed, unit(p, j, c))
                    act.activation(z_buf[:, c, :], z_buf[:, c, :], ACT.Sigmoid,
                                   bias=gate_bias[:, 1, c:c + 1]).then_inc(z_ready, 1)
                if not last and j >= UNITS - SETS:
                    split_first(p + 1, s)

            def candidate(p, j):
                for c in range(C):
                    act.wait_ge(cand_done, unit(p, j, c))
                    act.activation(cand[:, c, :], cand_ps[c][:, :], ACT.Tanh,
                                   bias=gate_bias[:, 2, c:c + 1]).then_inc(cand_ready, 1)

            split_first(0, 0)
            for m in range(M):
                prepare(m)
            take_first(0, 0)
            for i in range(M, EARLY):
                prepare(i)
            pairs(act, slot)
            candidate(PAIRS - 1, UNITS - 1)

        @block.vector
        def _(dve):
            def f32(ap):
                return ap.bitcast(F32)

            def low(dst, src, hi):
                return dve.tensor_tensor(dst, src, f32(hi), ALU.subtract)

            def statistics(p, s):
                dve.wait_ge(x_loaded[s], (p + 1) * 16)
                for m in range(M):
                    last = dve.bn_stats(stats[:, m, :], x_in[s][:, m, :])
                last.then_inc(mean_ready, 1)
                dve.wait_ge(mean_ready, once(p, s))
                dve.sem_inc(dve_passed, 1)
                for m in range(M):
                    last = dve.bn_aggr(mean_var[s][:, m, :], stats[:, m, :])
                last.then_inc(stats_ready, 1)

            def normalise(p, s):
                dve.wait_ge(rstd_ready, once(p, s))
                for m in range(M):
                    last = dve.tensor_scalar(h_first[s][:, m, :], x_in[s][:, m, :], mean_var[s][:, m, 0:1],
                                             rstd[s][:, m:m + 1], ALU.subtract, ALU.mult)
                last.then_inc(normed, 1)
                dve.wait_ge(normed, once(p, s))
                dve.tensor_scalar(h_first[s][:, :, :], h_first[s][:, :, :], 0.0, None, ALU.max).then_inc(h_first_ready, 1)

            def split_first(p, s):
                for t in range(2):
                    b = parts_of_bank(t)
                    dve.wait_ge(first_hi, graph(p, s, t))
                    low(hn_lo[s][:, b, :], h_first[s][:, b, :], hn_hi[s][:, b, :]).then_inc(first_lo, 1)

            def take_first(p, s):
                for c in range(C):
                    dve.wait_ge(hf_hi_ready, unit(p, s, c))
                    low(hf_lo[s][:, c, :], turned[c][:, :], hf_hi[s][:, c, :]).then_inc(hf_lo_ready, 1)

            def prepare(i):
                dve.wait_ge(prep_hi, i + 1)
                hi, lo = prep_parts(i)
                low(lo, bank[PREP_BANK[i]][:, :], hi).then_inc(prep_lo, 1)

            def take_next(p, j):
                s = j % SETS
                if j < SETS:
                    take_first(p, s)
                else:
                    for t in range(2):
                        b = parts_of_bank(t)
                        dve.wait_ge(hn_hi_ready, later(p, j, t))
                        low(hn_lo[s][:, b, :], turned[t][:, :].rearrange("p (b d) -> p b d", d=D),
                            hn_hi[s][:, b, :]).then_inc(hn_lo_ready, 1)

            def add_x(p, s):
                src = (turned, u_r)[s]
                dve.wait_ge(x_copied[s], 16 * (p + 1))
                for t in range(2):
                    b = parts_of_bank(t)
                    dve.wait_ge(last_turned, graph(p, s, t))
                    dve.tensor_tensor(x_out[s][:, b, :], src[t][:, :].rearrange("p (b d) -> p b d", d=D),
                                      x_out[s][:, b, :], ALU.add).then_inc(out_summed, 1)

            def new_h(p, j, c):
                s = j % SETS
                dve.wait_ge(cand_ready, unit(p, j, c))
                dve.tensor_tensor(cand[:, c, :], z_buf[:, c, :], cand[:, c, :], ALU.mult).then_inc(zc_ready, 1)
                dve.wait_ge(zc_ready, unit(p, j, c))
                dst = h_last[s] if j >= UNITS - SETS else hf[s]
                dve.tensor_tensor(dst[:, c, :], cand[:, c, :], keep[:, c, :], ALU.subtract).then_inc(h_ready, 1)

            def slot(p, j, first, last):
                s = j % SETS
                for c in range(C):
                    dve.wait_ge(a_hi_ready, unit(p, j, c))
                    low(a_lo[:, c, :], agg_z[c][:, :], a_hi[:, c, :]).then_inc(a_lo_ready, 1)
                if j == 0 and not first:
                    add_x(p - 1, 0)
                if first:
                    normalise(0, 1)
                    split_first(0, 1)
                    for i in range(EARLY, len(PREP) - 1):
                        prepare(i)
                    dve.wait_ge(bias_copied, 1)
                    for g, (b0, b1) in enumerate(((1, 0), (2, 0), (3, 4))):
                        dve.tensor_tensor(gate_bias[:, g, :], bias_cols[:, b0, :], bias_cols[:, b1, :],
                                          ALU.add).then_inc(bias_ready, 1)
                    prepare(len(PREP) - 1)
                if not first:
                    q = before(p, j)
                    for c in range(C):
                        new_h(*q, c)
                for c in range(C):
                    dve.wait_ge(u_copied, unit(p, j, c))
                    dve.wait_ge(r_done, unit(p, j, c))
                    dve.tensor_tensor(r_buf[:, c, :], u_r[c][:, :], u_kept[:, c, :], ALU.add).then_inc(r_summed, 1)
                if not first and q[1] < UNITS - SETS:
                    for c in range(C):
                        dve.wait_ge(hf_hi_ready, unit(q[0], q[1] + SETS, c))
                        low(hf_lo[1 - s][:, c, :], hf[1 - s][:, c, :], hf_hi[1 - s][:, c, :]).then_inc(hf_lo_ready, 1)
                for c in range(C):
                    dve.wait_ge(z_done, unit(p, j, c))
                    dve.tensor_tensor(z_buf[:, c, :], agg_z[c][:, :], u_kept[:, c, :], ALU.add).then_inc(z_summed, 1)
                if not (last and j == UNITS - 1):
                    take_next(*after(p, j))
                for c in range(C):
                    dve.wait_ge(r_ready, unit(p, j, c))
                    dve.tensor_tensor(rh[:, c, :], r_buf[:, c, :], hf[s][:, c, :], ALU.mult).then_inc(rh_ready, 1)
                for c in range(C):
                    dve.wait_ge(rh_hi_ready, unit(p, j, c))
                    low(rh_lo[:, c, :], rh[:, c, :], rh_hi[:, c, :]).then_inc(rh_lo_ready, 1)
                if j == 0 and not first:
                    add_x(p - 1, 1)
                for c in range(C):
                    dve.wait_ge(z_ready, unit(p, j, c))
                    dve.scalar_tensor_tensor(out=keep[:, c, :], in0=z_buf[:, c, :], scalar=1.0, in1=hf[s][:, c, :],
                                             op0=ALU.subtract, op1=ALU.mult).then_inc(keep_ready, 1)
                if not last and j >= UNITS - SETS:
                    normalise(p + 1, s)
                    split_first(p + 1, s)
                if not last and j in (UNITS - SETS - 1, UNITS - SETS):
                    statistics(p + 1, j - (UNITS - SETS - 1))

            statistics(0, 0)
            normalise(0, 0)
            split_first(0, 0)
            for m in range(M):
                prepare(m)
            take_first(0, 0)
            statistics(0, 1)
            for i in range(M, EARLY):
                prepare(i)
            pairs(dve, slot)
            for c in range(C):
                new_h(PAIRS - 1, UNITS - 1, c)
            for s in range(SETS):
                add_x(PAIRS - 1, s)


_INS = ["x", "adj", "L0_gnn_w3_w", "L0_gnn_w3_b", "L0_gnn_u3_w", "L0_gnn_u3_b", "L0_gnn_w4_w", "L0_gnn_w4_b",
        "L0_gnn_w5_w", "L0_gnn_w5_b", "L0_gnn_u5_w", "L0_gnn_u5_b"]


def kernel(**inputs):
    import numpy as np
    import concourse.bacc as bacc
    from concourse.bass_utils import run_bass_kernel_spmd

    nc = bacc.Bacc("TRN2", target_bir_lowering=False, num_devices=1)
    arrays, args = {}, []
    for name in _INS:
        a = np.ascontiguousarray(inputs[name])
        arrays[f"in_{name}"] = a
        args.append(nc.dram_tensor(f"in_{name}", a.shape, mybir.dt.from_np(a.dtype), kind="ExternalInput").ap())
    out = nc.dram_tensor("out", inputs["x"].shape, F32, kind="ExternalOutput").ap()
    gated_graph_network(nc, *args, out)
    result = run_bass_kernel_spmd(nc, [arrays], core_ids=[0])
    return result.results[0]["out"]
```
